# Optimizing a Trainium2 kernel written in Bass

```python
import numpy as np
import jax
import jax.numpy as jnp

def _softmax(x, axis=-1):
    return jax.nn.softmax(x, axis=axis)

def _gelu(x):
    return jax.nn.gelu(x, approximate=True)

def _silu(x):
    return jax.nn.silu(x)

def _sigmoid(x):
    return jax.nn.sigmoid(x)

def _layernorm(x, axis=-1, eps=1e-05):
    m = jnp.mean(x, axis=axis, keepdims=True)
    v = jnp.var(x, axis=axis, keepdims=True)
    return (x - m) / jnp.sqrt(v + eps)

def _scatter_add(tgt, idx, src, axis=0):
    return tgt.at[idx].add(src)

def _segment_sum(src, seg, n):
    return jax.ops.segment_sum(src, seg, n)
kernel_name = 'mk_adaln_ffn_d1_seqx_r4_acaa15'

def setup_inputs(seed: int=0):
    np.random.seed(seed)
    _w = jnp.asarray

    def _rec_inputs():
        import jax
        import jax.numpy as jnp
        _rk = jax.random.key(seed)
        x = -7.109e-05 + 0.9999 * jax.random.normal(jax.random.fold_in(_rk, 1), (128, 64, 1024), jnp.float32)
        _lenS = 64 - jax.random.randint(jax.random.fold_in(_rk, 7), (128,), 0, max(1, 64 // 4) + 1, jnp.int32)
        _lenS2 = 64 - jax.random.randint(jax.random.fold_in(_rk, 8), (128,), 0, max(1, 64 // 4) + 1, jnp.int32)
        itok_B_0_15 = jax.random.randint(jax.random.fold_in(_rk, 11), (128,), 0, 16, jnp.int32)
        return (x, itok_B_0_15)
    x, itok_B_0_15 = _rec_inputs()

    def _L0_cond_setup():
        import jax, jax.numpy as jnp
        import numpy as np
        NUM_CONDITIONS = 16
        IN_CH = 64
        OUT_CH = 64
        B = 64
        T = 1024
        key = jax.random.key(seed)
        k_x, k_w, k_c = jax.random.split(key, 3)
        x = jax.random.normal(k_x, (B, IN_CH, T), dtype=jnp.float32)
        bound = float(np.sqrt(6.0 / IN_CH))
        weights = jax.random.uniform(k_w, (NUM_CONDITIONS, IN_CH, OUT_CH), dtype=jnp.float32, minval=-bound, maxval=bound)
        condition = jax.random.randint(k_c, (B,), 0, NUM_CONDITIONS, dtype=jnp.int64)
        return {'x': x, 'weights': weights, 'condition': condition}
    _L0_cond_all = _L0_cond_setup()
    _L0_cond_in = {k: v for k, v in _L0_cond_all.items() if k in ('weights',)}
    del _L0_cond_all

    def _L0_ffn_setup():
        import jax, jax.numpy as jnp
        import numpy as np
        BATCH, SEQ, D = (2, 512, 1024)
        K, TOPK, RANK = (64, 16, 16)
        ALPHA = 32.0
        SCALING = ALPHA / RANK
        key = jax.random.key(seed)
        k1, k2, k3, k4 = jax.random.split(key, 4)
        x = jax.random.normal(k1, (BATCH, SEQ, D), dtype=jnp.float32)
        A = jax.random.normal(k2, (K, RANK, D), dtype=jnp.float32) * 0.02
        B = jax.random.normal(k3, (K, D, RANK), dtype=jnp.float32) * 0.02
        Wr = jax.random.normal(k4, (K, D), dtype=jnp.float32) * 0.02
        return {'x': x, 'A': A, 'B': B, 'Wr': Wr}
    _L0_ffn_all = _L0_ffn_setup()
    _L0_ffn_in = {k: v for k, v in _L0_ffn_all.items() if k in ('A', 'B', 'Wr')}
    del _L0_ffn_all
    return {'x': x, 'itok_B_0_15': itok_B_0_15, 'L0_cond_weights': _L0_cond_in['weights'], 'L0_ffn_A': _L0_ffn_in['A'], 'L0_ffn_B': _L0_ffn_in['B'], 'L0_ffn_Wr': _L0_ffn_in['Wr']}

def reference(x, itok_B_0_15, L0_cond_weights, L0_ffn_A, L0_ffn_B, L0_ffn_Wr):
    import jax
    import jax.numpy as jnp

    def _L0_cond_ref(x, weights, condition):
        import jax, jax.numpy as jnp
        import numpy as np
        NUM_CONDITIONS = 16
        IN_CH = 64
        OUT_CH = 64
        B = 64
        T = 1024
        W = weights[condition]
        return jnp.einsum('bct,bcd->bdt', x, W)

    def _L0_ffn_ref(x, A, B, Wr):
        import jax, jax.numpy as jnp
        import numpy as np
        BATCH, SEQ, D = (2, 512, 1024)
        K, TOPK, RANK = (64, 16, 16)
        ALPHA = 32.0
        SCALING = ALPHA / RANK
        prefix = x.shape[:-1]
        xf = x.reshape(-1, x.shape[-1])
        N = xf.shape[0]
        scores = xf @ Wr.T
        top_vals, top_idx = jax.lax.top_k(scores, TOPK)
        gates = jax.nn.softmax(top_vals, axis=-1)
        G = jnp.zeros((N, K), xf.dtype).at[jnp.arange(N)[:, None], top_idx].set(gates)
        h = jnp.einsum('nd,krd->nkr', xf, A)
        out = jnp.einsum('nkr,kdr->nd', h * G[:, :, None], B)
        return (out * SCALING).reshape(*prefix, -1)
    x = x + _L0_ffn_ref(_L0_cond_ref(x, L0_cond_weights, itok_B_0_15), L0_ffn_A, L0_ffn_B, L0_ffn_Wr)
    return x

_drawn_inputs = setup_inputs


def setup_inputs(seed=0):
    import zlib

    import numpy as np

    out = dict(_drawn_inputs(seed))
    spreads = {}
    factors = {}
    for name, (base, spread) in spreads.items():
        noise = np.random.default_rng([zlib.crc32(name.encode()), seed]).standard_normal(out[name].shape)
        drawn = base * np.exp(spread * noise) if base else spread * noise
        out[name] = jnp.asarray(drawn.astype(out[name].dtype))
    for name, factor in factors.items():
        out[name] = (out[name] * factor).astype(out[name].dtype)
    return out
```

```python
from contextlib import ExitStack

import concourse.bass as bass
from concourse import mybir

F32 = mybir.dt.float32
F32R = mybir.dt.float32r
I32 = mybir.dt.int32
ALU = mybir.AluOpType
ACT = mybir.ActivationFunctionType
AX_X = mybir.AxisListType.X

P = 128
BANK = 512
SCALING = 2.0
LOWEST = -3.4028234663852886e38


def conditioned_moe_kernel(nc, x, cond, w_cond, lora_a, lora_b, w_router, out):
    NB, C, D = x.shape
    NCOND = w_cond.shape[0]
    K, R, _ = lora_a.shape
    KR = K * R
    G = BANK
    TILES = G // P
    NG = NB * C // G
    BPT = P // C
    DC = D // P
    MC = KR // P
    KPM = P // R
    HALVES = D // BANK
    PAIRS = DC // 2
    XS = 2
    UM = 2
    UPT = MC // UM
    UNITS = TILES * UPT
    SPLITS = 4
    OUTS = TILES * HALVES
    OSLOTS = 4
    JB = 4
    TOP = 8
    assert K == P // 2 and BPT == 2 and DC == MC == 8 and HALVES == 2 and OUTS % OSLOTS == 0
    assert UNITS == 16 and PAIRS == 4

    x_rows = x.rearrange("b c t -> (b c) t")
    out_rows = out.rearrange("b c t -> (b c) t")

    with ExitStack() as ctx:
        def sb(name, shape, dt=F32):
            return ctx.enter_context(nc.sbuf_tensor(name, shape, dt))

        def sem(name):
            return ctx.enter_context(nc.semaphore(name))

        with nc.sbuf_tensor("b_stage", [P, MC, KPM, P], F32) as b_stage, \
                nc.sbuf_tensor("a_stage", [P, MC, D], F32) as a_stage:
            pass
        b_hi = sb("b_hi", [P, MC, D], F32R)
        b_lo = sb("b_lo", [P, MC, D], F32R)
        a_hi = sb("a_hi", [P, DC, KR], F32R)
        a_lo = sb("a_lo", [P, DC, KR], F32R)
        wr_t = sb("wr_t", [P, DC, P], F32R)
        y_hi = sb("y_hi", [P, DC, G], F32R)
        y_lo = sb("y_lo", [P, DC, G], F32R)
        p_t = sb("p_t", [P, MC, G])
        ps_hi = sb("ps_hi", [P, SPLITS, UM, P], F32R)
        ps_lo = sb("ps_lo", [P, SPLITS, UM, P], F32R)
        x_in = sb("x_in", [P, XS, TILES, 2 * P])
        io = sb("io", [P, OSLOTS, BANK])
        b_order = io[:, :, :].rearrange("p (s h) (j k r) -> p s (h j) k r", s=2, k=KPM, r=R)
        w_diag = sb("w_diag", [P, TILES, P])
        wr_in = sb("wr_in", [P, D])
        ident = sb("ident", [P, P])
        fold = sb("fold", [P, K])
        sg = sb("sg", [P, BANK])
        cond_sb = sb("cond_sb", [1, NB], I32)
        rows = sb("rows", [P, TILES, K])
        max1 = sb("max1", [P, TILES, TOP])
        max2 = sb("max2", [P, TILES, TOP])
        rest1 = sb("rest1", [P, TILES, K])
        rest2 = sb("rest2", [P, TILES, K])
        below = sb("below", [P, TILES, K])
        expd = sb("expd", [P, TILES, K])
        chosen = sb("chosen", [P, TILES, K])
        gates = sb("gates", [P, TILES, K])
        gates_n = sb("gates_n", [P, TILES, K])
        gsum = sb("gsum", [P, TILES])
        ginv = sb("ginv", [P, TILES])

        hb = ctx.enter_context(nc.psum_tensor("hb", [P, 2, BANK], F32))
        ob = ctx.enter_context(nc.psum_tensor("ob", [P, OSLOTS, BANK], F32))
        sb_bank = ctx.enter_context(nc.psum_tensor("sb_bank", [P, BANK], F32))
        tr_bank = ctx.enter_context(nc.psum_tensor("tr_bank", [P, BANK], F32))

        cleared = sem("cleared")
        consts = sem("consts")
        cond_in = sem("cond_in")
        wr_landed = sem("wr_landed")
        a_landed = [sem(f"a_landed{m}") for m in range(MC)]
        b_landed = [sem(f"b_landed{m}") for m in range(MC)]
        wr_ps = sem("wr_ps")
        wr_hid = sem("wr_hid")
        wr_lod = sem("wr_lod")
        b_ordered = sem("b_ordered")
        prep_ps = sem("prep_ps")
        prep_hi = sem("prep_hi")
        prep_lo = sem("prep_lo")
        w_landed = sem("w_landed")
        x_landed = [sem(f"x_landed{s}") for s in range(XS)]
        y_ps = sem("y_ps")
        y_hid = sem("y_hid")
        y_lod = sem("y_lod")
        s_ps = sem("s_ps")
        s_out = sem("s_out")
        st_ps = sem("st_ps")
        topk = sem("topk")
        exp_done = sem("exp_done")
        gt_ps = sem("gt_ps")
        gt_out = sem("gt_out")
        gx_landed = sem("gx_landed")
        h_ps = sem("h_ps")
        p_done = sem("p_done")
        sp_hi = sem("sp_hi")
        sp_lo = sem("sp_lo")
        sp_used = sem("sp_used")
        o_ps = sem("o_ps")
        o_done = sem("o_done")
        r_landed = [sem(f"r_landed{s}") for s in range(OSLOTS)]
        stored = [sem(f"stored{s}") for s in range(OSLOTS)]

        PREP = [("A", 0)] + [w for m in range(MC) for w in ([("A", m + 1)] if m + 1 < MC else []) + [("B", m)]]
        N_PREP = 2 * len(PREP)
        WR_BANKS = DC // JB
        GX_DMAS = 2 * MC

        MAX1, REST1, MAX2, REST2, BELOW, CHOSEN, WEIGHTED, SUMMED, INVERTED, GATED = range(1, 11)
        STEPS = GATED

        def turned(kind, m, half):
            if kind == "A":
                cs = slice(half * JB, (half + 1) * JB)
                return (a_hi[:, cs, m * P:(m + 1) * P], a_lo[:, cs, m * P:(m + 1) * P], "p (j q) -> p j q")
            js = slice(half * JB, (half + 1) * JB)
            return (b_hi[:, m, :].rearrange("p (q j) -> p q j", j=DC)[:, :, js],
                    b_lo[:, m, :].rearrange("p (q j) -> p q j", j=DC)[:, :, js], "p (j q) -> p q j")

        block = ctx.enter_context(nc.Block())

        @block.sync
        def _(sp):
            def load_cond_weights(g):
                if not isinstance(g, int) or g > 0:
                    sp.wait_ge(y_ps, DC * g)
                for t in range(TILES):
                    for h in range(BPT):
                        b = g * (TILES * BPT) + (t * BPT + h)
                        which = sp.value_load(cond_sb[0:1, bass.ds(b, 1)], min_val=0, max_val=NCOND - 1)
                        sp.dma_start(w_diag[h * C:(h + 1) * C, t, h * C:(h + 1) * C],
                                     w_cond[bass.ds(which, 1), :, :].rearrange("o c d -> (o c) d")
                                     ).then_inc(w_landed, 16)

            def load_x_pair(g, pair):
                if not isinstance(g, int) or g > 0 or pair >= XS:
                    sp.wait_ge(y_ps, DC * g + 2 * (pair - XS) + 2)
                sp.dma_start(x_in[:, pair % XS, :, :],
                             x_rows[bass.ds(g * G, G), pair * 2 * P:(pair + 1) * 2 * P]
                             .rearrange("(t p) d -> p t d", p=P)).then_inc(x_landed[pair % XS], 16)

            def piece(rows, g, k):
                t, half = k // HALVES, k % HALVES
                return rows[bass.ds(g * G + t * P, P), half * BANK:(half + 1) * BANK]

            def load_residual(g, k):
                slot, uses = k % OSLOTS, (OUTS // OSLOTS) * g + k // OSLOTS
                if not isinstance(uses, int) or uses > 0:
                    sp.wait_ge(stored[slot], 16 * uses)
                sp.dma_start(io[:, slot, :], piece(x_rows, g, k)).then_inc(r_landed[slot], 16)

            def store(g, k):
                sp.wait_ge(o_done, OUTS * g + (k + 1))
                sp.dma_start(piece(out_rows, g, k), io[:, k % OSLOTS, :]).then_inc(stored[k % OSLOTS], 16)

            def spread_gates(g, half):
                sp.wait_ge(gt_out, g + 1)
                if not isinstance(g, int) or g > 0:
                    sp.wait_ge(sp_lo, UNITS * g - UNITS + (half + 1) * (UNITS // 2))
                for m in range(MC):
                    rows = slice(half * K + m * KPM, half * K + (m + 1) * KPM)
                    src = sg[rows, 0:2 * P].unsqueeze(1).broadcast_to([KPM, R, 2 * P])
                    sp.dma_start(p_t[:, m, half * 2 * P:(half + 1) * 2 * P], src).then_inc(gx_landed, 16)

            def steady(g, ahead):
                if ahead:
                    load_cond_weights(g + 1)
                    load_x_pair(g + 1, 0)
                    load_x_pair(g + 1, 1)
                if isinstance(g, int) and g == 0:
                    sp.wait_ge(prep_ps, N_PREP)
                for k in range(OSLOTS):
                    load_residual(g, k)
                if ahead:
                    load_x_pair(g + 1, 2)
                    load_x_pair(g + 1, 3)
                for t in range(TILES):
                    if ahead and t >= 2:
                        spread_gates(g + 1, t - 2)
                    store(g, 2 * t)
                    store(g, 2 * t + 1)
                    if t < 2:
                        load_residual(g, 2 * t + OSLOTS)
                        load_residual(g, 2 * t + 1 + OSLOTS)

            sp.dma_start(cond_sb[0:1, :], cond.rearrange("(o b) -> o b", o=1)).then_inc(cond_in, 16)
            load_x_pair(0, 0)
            sp.wait_ge(cond_in, 16)
            sp.wait_ge(consts, 3)
            load_cond_weights(0)
            load_x_pair(0, 1)
            load_x_pair(0, 2)
            load_x_pair(0, 3)
            spread_gates(0, 0)
            spread_gates(0, 1)
            steady(0, True)
            with sp.Fori(1, NG - 1) as g:
                steady(g, True)
            steady(NG - 1, False)
            for slot in range(OSLOTS):
                sp.wait_ge(stored[slot], 16 * NG * OUTS // OSLOTS)

        @block.gpsimd
        def _(pool):
            nc.gpsimd.memset(ident[:, :], 0.0).then_inc(cleared, 1)
            nc.gpsimd.memset(fold[:, :], 0.0).then_inc(cleared, 1)
            nc.gpsimd.memset(w_diag[:, :, :], 0.0).then_inc(consts, 1)
            pool.wait_ge(cleared, 2)
            nc.gpsimd.affine_select(out=ident[:, :], in_=ident[:, :], compare_op=ALU.not_equal, fill=1.0,
                                    base=0, pattern=[[-1, P]], channel_multiplier=1).then_inc(consts, 1)
            nc.gpsimd.affine_select(out=fold[:, :], in_=fold[:, :], compare_op=ALU.not_equal, fill=1.0,
                                    base=0, pattern=[[-1, K]], channel_multiplier=1).then_inc(cleared, 1)
            pool.wait_ge(cleared, 3)
            nc.gpsimd.affine_select(out=fold[:, :], in_=fold[:, :], compare_op=ALU.not_equal, fill=1.0,
                                    base=-K, pattern=[[-1, K]], channel_multiplier=1).then_inc(consts, 1)
            for m in range(MC):
                pool.wait_ge(b_landed[m], 16)
                if m >= 2:
                    pool.wait_ge(prep_ps, 2 * PREP.index(("B", m - 2)) + 2)
                nc.gpsimd.tensor_copy(b_order[:, m % 2, :, :, :],
                                      b_stage[:, m, :, :].rearrange("p k (j r) -> p j k r", r=R)
                                      ).then_inc(b_ordered, 1)

        @block.scalar
        def _(act):
            def load_weights():
                for h in range(2):
                    act.dma_start(wr_in[h * K:(h + 1) * K, :], w_router).then_inc(wr_landed, 16)
                a_rows = lora_a.rearrange("k r d -> (k r) d")
                for kind, m in PREP:
                    if kind == "A":
                        act.dma_start(a_stage[:, m, :], a_rows[m * P:(m + 1) * P, :]).then_inc(a_landed[m], 16)
                    else:
                        act.dma_start(b_stage[:, m, :, :], lora_b[m * KPM:(m + 1) * KPM, :, :]
                                      .rearrange("k (p j) r -> p k (j r)", p=P)).then_inc(b_landed[m], 16)

            def router_hi(i):
                act.wait_ge(wr_ps, i + 1)
                nc.scalar.activation(wr_t[:, i * JB:(i + 1) * JB, 0:K],
                                     hb[:, i, :].rearrange("p (j q) -> p j q", j=JB)[:, :, 0:K],
                                     ACT.Copy).then_inc(wr_hid, 1)

            def weights_hi(n):
                kind, m = PREP[n]
                for half in range(2):
                    q = 2 * n + half
                    act.wait_ge(prep_ps, q + 1)
                    hi, _, order = turned(kind, m, half)
                    nc.scalar.activation(hi, ob[:, q % OSLOTS, :].rearrange(order, j=JB),
                                         ACT.Copy).then_inc(prep_hi, 1)

            def y_hi_part(g, c):
                act.wait_ge(y_ps, DC * g + (c + 1))
                nc.scalar.activation(y_hi[:, c, :], ob[:, c % OSLOTS, :], ACT.Copy).then_inc(y_hid, 1)

            def split_hi(g, u):
                t, ms = u // UPT, (u % UPT) * UM
                act.wait_ge(p_done, MC * g + (ms + UM))
                if not isinstance(g, int) or g > 0 or u >= SPLITS:
                    act.wait_ge(sp_used, UNITS * g + (u + 1 - SPLITS))
                nc.scalar.activation(ps_hi[:, u % SPLITS, :, :], p_t[:, ms:ms + UM, t * P:(t + 1) * P],
                                     ACT.Copy).then_inc(sp_hi, 1)

            def scores_out(g):
                act.wait_ge(s_ps, g + 1)
                if not isinstance(g, int) or g > 0:
                    act.wait_ge(gx_landed, 16 * GX_DMAS * g)
                nc.scalar.activation(sg[:, :], sb_bank[:, :], ACT.Copy).then_inc(s_out, 1)

            def exponentials(g):
                act.wait_ge(topk, STEPS * g + BELOW)
                nc.scalar.activation(expd[:, :, :], below[:, :, :], ACT.Exp).then_inc(exp_done, 1)

            def gates_out(g):
                act.wait_ge(gt_ps, g + 1)
                nc.scalar.activation(sg[:, 0:2 * P], sb_bank[:, 0:2 * P], ACT.Copy).then_inc(gt_out, 1)

            def steady(g, ahead):
                for c in range(DC):
                    if ahead:
                        y_hi_part(g + 1, c)
                    if c < SPLITS:
                        split_hi(g, c)
                if ahead:
                    scores_out(g + 1)
                for u in range(UNITS):
                    if u + SPLITS < UNITS:
                        split_hi(g, u + SPLITS)
                    if ahead and u == 4:
                        exponentials(g + 1)
                    if ahead and u == 8:
                        gates_out(g + 1)

            load_weights()
            for i in range(WR_BANKS):
                router_hi(i)
            for c in range(DC):
                y_hi_part(0, c)
            weights_hi(0)
            scores_out(0)
            weights_hi(1)
            exponentials(0)
            gates_out(0)
            for n in range(2, len(PREP)):
                weights_hi(n)
            steady(0, True)
            with act.Fori(1, NG - 1) as g:
                steady(g, True)
            steady(NG - 1, False)

        @block.vector
        def _(dve):
            def router_lo(i):
                dve.wait_ge(wr_hid, i + 1)
                cs = slice(i * JB, (i + 1) * JB)
                nc.vector.tensor_tensor(wr_t[:, cs, K:2 * K],
                                        hb[:, i, :].rearrange("p (j q) -> p j q", j=JB)[:, :, K:2 * K],
                                        wr_t[:, cs, 0:K].bitcast(F32), ALU.subtract).then_inc(wr_lod, 1)

            def weights_lo(n):
                kind, m = PREP[n]
                for half in range(2):
                    q = 2 * n + half
                    dve.wait_ge(prep_hi, q + 1)
                    hi, lo, order = turned(kind, m, half)
                    nc.vector.tensor_tensor(lo, ob[:, q % OSLOTS, :].rearrange(order, j=JB),
                                            hi.bitcast(F32), ALU.subtract).then_inc(prep_lo, 1)

            def y_lo_part(g, c):
                dve.wait_ge(y_hid, DC * g + (c + 1))
                nc.vector.tensor_tensor(y_lo[:, c, :], ob[:, c % OSLOTS, :], y_hi[:, c, :].bitcast(F32),
                                        ALU.subtract).then_inc(y_lod, 1)

            def gate_rows(g, m):
                if m == 0:
                    dve.wait_ge(gx_landed, 16 * GX_DMAS * (g + 1))
                dve.wait_ge(h_ps, MC * g + (m + 1))
                nc.vector.tensor_tensor(p_t[:, m, :], hb[:, m % 2, :], p_t[:, m, :],
                                        ALU.mult).then_inc(p_done, 1)

            def split_lo(g, u):
                t, ms = u // UPT, (u % UPT) * UM
                dve.wait_ge(sp_hi, UNITS * g + (u + 1))
                nc.vector.tensor_tensor(ps_lo[:, u % SPLITS, :, :], p_t[:, ms:ms + UM, t * P:(t + 1) * P],
                                        ps_hi[:, u % SPLITS, :, :].bitcast(F32),
                                        ALU.subtract).then_inc(sp_lo, 1)

            def add_residual(g, k):
                slot = k % OSLOTS
                if k % HALVES == 0:
                    dve.wait_ge(o_ps, TILES * g + (k // HALVES + 1))
                else:
                    dve.wait_ge(sp_used, UNITS * g + UPT * (k // HALVES + 1))
                dve.wait_ge(r_landed[slot], 16 * ((OUTS // OSLOTS) * g + (k // OSLOTS + 1)))
                nc.vector.scalar_tensor_tensor(out=io[:, slot, :], in0=ob[:, slot, :], scalar=SCALING,
                                               in1=io[:, slot, :], op0=ALU.mult,
                                               op1=ALU.add).then_inc(o_done, 1)

            scores = tr_bank[:, 0:TILES * K].rearrange("p (t k) -> p t k", k=K)

            def per_row(a):
                return a.unsqueeze(2).broadcast_to([P, TILES, K])

            def gating(g, step):
                if step == MAX1:
                    dve.wait_ge(st_ps, g + 1)
                    nc.vector.tensor_copy(rows[:, :, :], scores)
                    dve.drain()
                    for t in range(TILES):
                        last = nc.vector.max(max1[:, t, :], rows[:, t, :])
                elif step == REST1:
                    dve.drain()
                    for t in range(TILES):
                        last = nc.vector.match_replace(rest1[:, t, :], max1[:, t, :], rows[:, t, :], LOWEST)
                elif step == MAX2:
                    dve.drain()
                    for t in range(TILES):
                        last = nc.vector.max(max2[:, t, :], rest1[:, t, :])
                elif step == REST2:
                    dve.drain()
                    for t in range(TILES):
                        last = nc.vector.match_replace(rest2[:, t, :], max2[:, t, :], rest1[:, t, :], LOWEST)
                elif step == BELOW:
                    last = nc.vector.tensor_tensor(below[:, :, :], rows[:, :, :], per_row(max1[:, :, 0]), ALU.subtract)
                elif step == CHOSEN:
                    dve.wait_ge(topk, STEPS * g + REST2)
                    last = nc.vector.tensor_tensor(chosen[:, :, :], rest2[:, :, :], rows[:, :, :], ALU.is_lt)
                elif step == WEIGHTED:
                    dve.wait_ge(exp_done, g + 1)
                    dve.wait_ge(topk, STEPS * g + CHOSEN)
                    last = nc.vector.tensor_tensor(gates[:, :, :], expd[:, :, :], chosen[:, :, :], ALU.mult)
                elif step == SUMMED:
                    dve.wait_ge(topk, STEPS * g + WEIGHTED)
                    last = nc.vector.reduce_sum(gsum[:, :], gates[:, :, :], AX_X)
                elif step == INVERTED:
                    dve.wait_ge(topk, STEPS * g + SUMMED)
                    last = nc.vector.reciprocal(ginv[:, :], gsum[:, :])
                elif step == GATED:
                    dve.wait_ge(topk, STEPS * g + INVERTED)
                    last = nc.vector.tensor_tensor(
                        gates_n[:, :, :].rearrange("p (b a) k -> p a b k", a=2),
                        gates[:, :, :].rearrange("p (a b) k -> p a b k", a=2),
                        per_row(ginv[:, :]).rearrange("p (a b) k -> p a b k", a=2), ALU.mult)
                last.then_inc(topk, 1)

            def steady(g, ahead, gated=False):
                if not gated:
                    for m in range(MC):
                        gate_rows(g, m)
                for c in range(DC):
                    if ahead:
                        y_lo_part(g + 1, c)
                    if c < SPLITS:
                        split_lo(g, c)
                for u in range(UNITS):
                    if u + SPLITS < UNITS:
                        split_lo(g, u + SPLITS)
                    if ahead and 2 <= u <= 6:
                        gating(g + 1, 2 * (u - 2) + 1)
                        gating(g + 1, 2 * (u - 2) + 2)
                    if u % UPT == UPT - 1:
                        for half in range(HALVES):
                            add_residual(g, HALVES * (u // UPT) + half)

            for i in range(WR_BANKS):
                router_lo(i)
            for c in range(DC):
                y_lo_part(0, c)
            weights_lo(0)
            for step in range(1, BELOW + 1):
                gating(0, step)
            weights_lo(1)
            for step in range(BELOW + 1, STEPS + 1):
                gating(0, step)
            weights_lo(2)
            for m in range(MC):
                for n in range(3 + 2 * m, min(5 + 2 * m, len(PREP))):
                    weights_lo(n)
                gate_rows(0, m)
            steady(0, True, gated=True)
            with dve.Fori(1, NG - 1) as g:
                steady(g, True)
            steady(NG - 1, False)

        @block.tensor
        def _(pe):
            def turn_router(i):
                for j in range(JB):
                    c = i * JB + j
                    last = nc.tensor.transpose(hb[:, i, j * P:(j + 1) * P], wr_in[:, c * P:(c + 1) * P],
                                               ident[:, :])
                last.then_inc(wr_ps, 1)

            def turn_weights(n):
                kind, m = PREP[n]
                if kind == "A":
                    pe.wait_ge(a_landed[m], 16)
                else:
                    pe.wait_ge(b_ordered, m + 1)
                for half in range(2):
                    q = 2 * n + half
                    if q < OSLOTS:
                        pe.wait_ge(y_lod, DC)
                    else:
                        pe.wait_ge(prep_lo, q - OSLOTS + 1)
                    for j in range(JB):
                        c = half * JB + j
                        src = a_stage[:, m, c * P:(c + 1) * P] if kind == "A" else \
                            b_order[:, m % 2, c, :, :].rearrange("p k r -> p (k r)")
                        last = nc.tensor.transpose(ob[:, q % OSLOTS, j * P:(j + 1) * P], src, ident[:, :])
                    last.then_inc(prep_ps, 1)

            def condition(g, c):
                pair = c // 2
                if c == 0:
                    pe.wait_ge(w_landed, 16 * TILES * BPT * (g + 1))
                if c % 2 == 0:
                    pe.wait_ge(x_landed[pair % XS], 16 * ((PAIRS // XS) * g + (pair // XS + 1)))
                if c >= OSLOTS:
                    pe.wait_ge(y_lod, DC * g + (c + 1 - OSLOTS))
                elif not isinstance(g, int) or g > 1:
                    pe.wait_ge(o_done, OUTS * g - OUTS + (c + 1 - OSLOTS))
                for t in range(TILES):
                    last = nc.tensor.matmul(ob[:, c % OSLOTS, t * P:(t + 1) * P],
                                            x_in[:, pair % XS, t, (c % 2) * P:(c % 2 + 1) * P],
                                            w_diag[:, t, :], start=True, stop=True)
                last.then_inc(y_ps, 1)

            def route(g, c):
                pe.wait_ge(y_hid, DC * g + (c + 1))
                if c == 0 and (not isinstance(g, int) or g > 0):
                    pe.wait_ge(gt_out, g)
                nc.tensor.matmul(sb_bank[:, :], wr_t[:, c, :], y_hi[:, c, :], start=(c == 0), stop=False)
                pe.wait_ge(y_lod, DC * g + (c + 1))
                last = nc.tensor.matmul(sb_bank[:, :], wr_t[:, c, :], y_lo[:, c, :], start=False,
                                        stop=(c == DC - 1))
                if c == DC - 1:
                    last.then_inc(s_ps, 1)

            def condition_and_route(g):
                LAG = 2
                for c in range(DC + LAG):
                    if c < DC:
                        condition(g, c)
                    if c >= LAG:
                        route(g, c - LAG)

            def scores_by_rows(g):
                pe.wait_ge(s_out, g + 1)
                for t in range(TILES):
                    last = nc.tensor.matmul(tr_bank[:, t * K:(t + 1) * K], sg[:, t * P:(t + 1) * P], fold[:, :],
                                            start=True, stop=True)
                last.then_inc(st_ps, 1)

            def turn_gates(g):
                pe.wait_ge(topk, STEPS * (g + 1))
                for t in range(2):
                    last = nc.tensor.transpose(sb_bank[:, t * P:(t + 1) * P], 
                                               gates_n[:, 2 * t:2 * t + 2, :].rearrange("p t k -> p (t k)"),
                                               ident[:, :])
                last.then_inc(gt_ps, 1)

            def up(g, m):
                n = MC * g + m
                if not isinstance(n, int) or n >= 2:
                    pe.wait_ge(p_done, n - 1)
                ms = slice(m * P, (m + 1) * P)
                for c in range(DC):
                    for i, (w, y) in enumerate(((a_lo, y_hi), (a_hi, y_lo), (a_hi, y_hi))):
                        last = nc.tensor.matmul(hb[:, m % 2, :], w[:, c, ms], y[:, c, :],
                                                start=(c == 0 and i == 0), stop=(c == DC - 1 and i == 2))
                last.then_inc(h_ps, 1)

            def down(g, u):
                t, mu, slot = u // UPT, u % UPT, u % SPLITS
                pe.wait_ge(sp_lo, UNITS * g + (u + 1))
                for half in range(HALVES):
                    k = HALVES * t + half
                    if mu == 0 and (not isinstance(g, int) or OUTS * g + k >= OSLOTS):
                        pe.wait_ge(o_done, OUTS * g + (k + 1 - OSLOTS))
                    ds = slice(half * BANK, (half + 1) * BANK)
                    for i in range(UM):
                        m = mu * UM + i
                        for j, (p, b) in enumerate(((ps_lo, b_hi), (ps_hi, b_lo), (ps_hi, b_hi))):
                            last = nc.tensor.matmul(ob[:, k % OSLOTS, :], p[:, slot, i, :], b[:, m, ds],
                                                    start=(m == 0 and j == 0), stop=(m == MC - 1 and j == 2))
                    if mu == UPT - 1 and half == 0:
                        last.then_inc(o_ps, 1)
                last.then_inc(sp_used, 1)

            def steady(g, ahead, upped=False):
                if not upped:
                    for m in range(MC):
                        up(g, m)
                if ahead:
                    condition_and_route(g + 1)
                for u in range(UNITS):
                    down(g, u)
                    if ahead and u == 1:
                        scores_by_rows(g + 1)
                    if ahead and u == 7:
                        turn_gates(g + 1)

            pe.wait_ge(consts, 3)
            pe.wait_ge(wr_landed, 32)
            for i in range(WR_BANKS):
                turn_router(i)
            pe.wait_ge(wr_lod, WR_BANKS)
            condition_and_route(0)
            turn_weights(0)
            scores_by_rows(0)
            turn_weights(1)
            turn_gates(0)
            turn_weights(2)
            for m in range(MC):
                for n in range(3 + 2 * m, min(5 + 2 * m, len(PREP))):
                    turn_weights(n)
                pe.wait_ge(prep_lo, 2 * PREP.index(("A", m)) + 2)
                up(0, m)
            pe.wait_ge(prep_lo, N_PREP)
            steady(0, True, upped=True)
            with pe.Fori(1, NG - 1) as g:
                steady(g, True)
            steady(NG - 1, False)


_INS = ["x", "itok_B_0_15", "L0_cond_weights", "L0_ffn_A", "L0_ffn_B", "L0_ffn_Wr"]


def kernel(**inputs):
    import numpy as _np
    import concourse.bacc as _bacc
    from concourse import mybir as _mybir
    from concourse.bass_utils import run_bass_kernel_spmd as _run

    nc = _bacc.Bacc("TRN2", target_bir_lowering=False, num_devices=1, dynamic_dma_scratch_size=1024)
    arrays, args = {}, []
    for name in _INS:
        a = _np.ascontiguousarray(inputs[name])
        arrays[f"in_{name}"] = a
        args.append(nc.dram_tensor(f"in_{name}", a.shape, _mybir.dt.from_np(a.dtype), kind="ExternalInput").ap())
    out = nc.dram_tensor("out", inputs["x"].shape, _mybir.dt.float32, kind="ExternalOutput").ap()
    conditioned_moe_kernel(nc, *args, out)
    r = _run(nc, [arrays], core_ids=[0])
    return r.results[0]["out"]
```

```python
from contextlib import ExitStack

import concourse.bass as bass
from concourse import mybir

F32 = mybir.dt.float32
F32R = mybir.dt.float32r
I32 = mybir.dt.int32
ALU = mybir.AluOpType
ACT = mybir.ActivationFunctionType
AX_X = mybir.AxisListType.X

P = 128
BANK = 512
SCALING = 2.0
LOWEST = -3.4028234663852886e38


def conditioned_moe_kernel(nc, x, cond, w_cond, lora_a, lora_b, w_router, out):
    NB, C, D = x.shape
    NCOND = w_cond.shape[0]
    K, R, _ = lora_a.shape
    KR = K * R
    G = BANK
    TILES = G // P
    NG = NB * C // G
    BPT = P // C
    DC = D // P
    MC = KR // P
    KPM = P // R
    HALVES = D // BANK
    PAIRS = DC // 2
    UM = 2
    UPT = MC // UM
    UNITS = TILES * UPT
    SPLITS = 4
    OUTS = TILES * HALVES
    OSLOTS = 4
    JB = 4
    TOP = 8
    assert K == P // 2 and BPT == 2 and DC == MC == 8 and HALVES == 2 and OUTS % OSLOTS == 0
    assert UNITS == 16 and PAIRS == 4

    x_rows = x.rearrange("b c t -> (b c) t")
    out_rows = out.rearrange("b c t -> (b c) t")

    with ExitStack() as ctx:
        def sb(name, shape, dt=F32):
            return ctx.enter_context(nc.sbuf_tensor(name, shape, dt))

        def sem(name):
            return ctx.enter_context(nc.semaphore(name))

        with nc.sbuf_tensor("b_stage", [P, MC, KPM, P], F32) as b_stage, \
                nc.sbuf_tensor("a_stage", [P, MC, D], F32) as a_stage, \
                nc.sbuf_tensor("wr_stage", [P, D], F32) as wr_stage:
            pass
        b_hi = sb("b_hi", [P, MC, D], F32R)
        b_lo = sb("b_lo", [P, MC, D], F32R)
        a_hi = sb("a_hi", [P, DC, KR], F32R)
        a_lo = sb("a_lo", [P, DC, KR], F32R)
        wr_t = sb("wr_t", [P, DC, P], F32R)
        y_hi = sb("y_hi", [P, DC, G], F32R)
        y_lo = sb("y_lo", [P, DC, G], F32R)
        p_t = sb("p_t", [P, MC, G])
        ps_hi = sb("ps_hi", [P, SPLITS, UM, P], F32R)
        ps_lo = sb("ps_lo", [P, SPLITS, UM, P], F32R)
        x_in = sb("x_in", [P, PAIRS, TILES, 2 * P])
        io = sb("io", [P, OSLOTS, BANK])
        b_order = io[:, :, :].rearrange("p (s h) (j k r) -> p s (h j) k r", s=2, k=KPM, r=R)
        w_diag = sb("w_diag", [P, TILES, P])
        ident = sb("ident", [P, P])
        fold = sb("fold", [P, K])
        sg = sb("sg", [P, BANK])
        cond_sb = sb("cond_sb", [1, NB], I32)
        rows = sb("rows", [P, TILES, K])
        max1 = sb("max1", [P, TILES, TOP])
        max2 = sb("max2", [P, TILES, TOP])
        rest1 = sb("rest1", [P, TILES, K])
        rest2 = sb("rest2", [P, TILES, K])
        below = sb("below", [P, TILES, K])
        gates_n = sb("gates_n", [P, TILES, K])
        gsum = sb("gsum", [P, TILES])
        ginv = sb("ginv", [P, TILES])

        hb = ctx.enter_context(nc.psum_tensor("hb", [P, 2, BANK], F32))
        ob = ctx.enter_context(nc.psum_tensor("ob", [P, OSLOTS, BANK], F32))
        sb_bank = ctx.enter_context(nc.psum_tensor("sb_bank", [P, BANK], F32))
        tr_bank = ctx.enter_context(nc.psum_tensor("tr_bank", [P, BANK], F32))

        cleared = sem("cleared")
        consts = sem("consts")
        w_zeroed = sem("w_zeroed")
        cond_in = sem("cond_in")
        wr_landed = sem("wr_landed")
        a_landed = [sem(f"a_landed{m}") for m in range(MC)]
        b_landed = [sem(f"b_landed{m}") for m in range(MC)]
        wr_ps = sem("wr_ps")
        wr_hid = sem("wr_hid")
        wr_lod = sem("wr_lod")
        b_ordered = sem("b_ordered")
        prep_ps = sem("prep_ps")
        prep_hi = sem("prep_hi")
        prep_lo = sem("prep_lo")
        w_landed = sem("w_landed")
        x_landed = [sem(f"x_landed{i}") for i in range(PAIRS)]
        y_ps = sem("y_ps")
        y_hid = sem("y_hid")
        y_lod = sem("y_lod")
        s_ps = sem("s_ps")
        s_out = sem("s_out")
        st_ps = sem("st_ps")
        topk = sem("topk")
        exp_done = sem("exp_done")
        gt_ps = sem("gt_ps")
        gt_out = sem("gt_out")
        gx_landed = [sem(f"gx_landed{m}") for m in range(MC)]
        h_ps = sem("h_ps")
        p_done = sem("p_done")
        sp_hi = sem("sp_hi")
        sp_lo = sem("sp_lo")
        sp_used = sem("sp_used")
        o_ps = sem("o_ps")
        o_done = sem("o_done")
        r_landed = [sem(f"r_landed{s}") for s in range(OSLOTS)]
        stored = [sem(f"stored{s}") for s in range(OSLOTS)]

        PREP = [("A", 0), ("A", 1)] + [w for m in range(MC) for w in
                                       ([("A", m + 2)] if m + 2 < MC else []) + [("B", m)]]
        EARLY = 4
        N_PREP = 2 * len(PREP)
        WR_BANKS = DC // JB

        MAX1, REST1, MAX2, REST2, BELOW, CHOSEN, WEIGHTED, SUMMED, INVERTED, GATED = range(1, 11)
        STEPS = GATED

        def turned(kind, m, half):
            if kind == "A":
                cs = slice(half * JB, (half + 1) * JB)
                return (a_hi[:, cs, m * P:(m + 1) * P], a_lo[:, cs, m * P:(m + 1) * P], "p (j q) -> p j q")
            js = slice(half * JB, (half + 1) * JB)
            return (b_hi[:, m, :].rearrange("p (q j) -> p q j", j=DC)[:, :, js],
                    b_lo[:, m, :].rearrange("p (q j) -> p q j", j=DC)[:, :, js], "p (j q) -> p q j")

        block = ctx.enter_context(nc.Block())

        @block.sync
        def _(sp):
            def load_cond_weights(g):
                if not isinstance(g, int) or g > 0:
                    sp.wait_ge(y_ps, DC * g)
                for t in range(TILES):
                    for h in range(BPT):
                        b = g * (TILES * BPT) + (t * BPT + h)
                        which = sp.value_load(cond_sb[0:1, bass.ds(b, 1)], min_val=0, max_val=NCOND - 1)
                        sp.dma_start(w_diag[h * C:(h + 1) * C, t, h * C:(h + 1) * C],
                                     w_cond[bass.ds(which, 1), :, :].rearrange("o c d -> (o c) d")
                                     ).then_inc(w_landed, 16)

            def load_x_pair(g, pair):
                if not isinstance(g, int) or g > 0:
                    sp.wait_ge(y_ps, DC * g + (2 * pair + 2 - DC))
                sp.dma_start(x_in[:, pair, :, :],
                             x_rows[bass.ds(g * G, G), pair * 2 * P:(pair + 1) * 2 * P]
                             .rearrange("(t p) d -> p t d", p=P)).then_inc(x_landed[pair], 16)

            def load_weights():
                a_rows = lora_a.rearrange("k r d -> (k r) d")
                for kind, m in PREP:
                    if kind == "A":
                        sp.dma_start(a_stage[:, m, :], a_rows[m * P:(m + 1) * P, :]).then_inc(a_landed[m], 16)
                    else:
                        sp.dma_start(b_stage[:, m, :, :], lora_b[m * KPM:(m + 1) * KPM, :, :]
                                      .rearrange("k (p j) r -> p k (j r)", p=P)).then_inc(b_landed[m], 16)

            def piece(rows, g, k):
                t, half = k // HALVES, k % HALVES
                return rows[bass.ds(g * G + t * P, P), half * BANK:(half + 1) * BANK]

            def load_residual(g, k):
                slot, uses = k % OSLOTS, (OUTS // OSLOTS) * g + k // OSLOTS
                if not isinstance(uses, int) or uses > 0:
                    sp.wait_ge(stored[slot], 16 * uses)
                sp.dma_start(io[:, slot, :], piece(x_rows, g, k)).then_inc(r_landed[slot], 16)

            def store(g, k):
                sp.wait_ge(o_done, OUTS * g + (k + 1))
                sp.dma_start(piece(out_rows, g, k), io[:, k % OSLOTS, :]).then_inc(stored[k % OSLOTS], 16)

            def spread_gates(g, half, ms=range(MC)):
                sp.wait_ge(gt_out, g + 1)
                if not isinstance(g, int) or g > 0:
                    sp.wait_ge(sp_lo, UNITS * g - UNITS + (half + 1) * (UNITS // 2))
                for m in ms:
                    rows = slice(half * K + m * KPM, half * K + (m + 1) * KPM)
                    src = sg[rows, 0:2 * P].unsqueeze(1).broadcast_to([KPM, R, 2 * P])
                    sp.dma_start(p_t[:, m, half * 2 * P:(half + 1) * 2 * P], src).then_inc(gx_landed[m], 16)

            def steady(g, ahead):
                if ahead:
                    load_cond_weights(g + 1)
                    for pair in range(PAIRS):
                        load_x_pair(g + 1, pair)
                if isinstance(g, int) and g == 0:
                    sp.wait_ge(prep_ps, N_PREP)
                for k in range(OSLOTS):
                    load_residual(g, k)
                for t in range(TILES):
                    if ahead and t >= 2:
                        spread_gates(g + 1, t - 2)
                    store(g, 2 * t)
                    store(g, 2 * t + 1)
                    if t < 2:
                        load_residual(g, 2 * t + OSLOTS)
                        load_residual(g, 2 * t + 1 + OSLOTS)

            sp.dma_start(cond_sb[0:1, :], cond.rearrange("(o b) -> o b", o=1)).then_inc(cond_in, 16)
            for h in range(2):
                sp.dma_start(wr_stage[h * K:(h + 1) * K, :], w_router).then_inc(wr_landed, 16)
            load_x_pair(0, 0)
            sp.wait_ge(cond_in, 16)
            sp.wait_ge(w_zeroed, 1)
            load_cond_weights(0)
            for pair in range(1, PAIRS):
                load_x_pair(0, pair)
            load_weights()
            for m in range(MC):
                for half in range(2):
                    spread_gates(0, half, [m])
            steady(0, True)
            with sp.Fori(1, NG - 1) as g:
                steady(g, True)
            steady(NG - 1, False)
            for slot in range(OSLOTS):
                sp.wait_ge(stored[slot], 16 * NG * OUTS // OSLOTS)

        @block.gpsimd
        def _(pool):
            nc.gpsimd.memset(ident[:, :], 0.0).then_inc(cleared, 1)
            nc.gpsimd.memset(fold[:, :], 0.0).then_inc(cleared, 1)
            pool.wait_ge(cleared, 2)
            nc.gpsimd.affine_select(out=ident[:, :], in_=ident[:, :], compare_op=ALU.not_equal, fill=1.0,
                                    base=0, pattern=[[-1, P]], channel_multiplier=1).then_inc(consts, 1)
            nc.gpsimd.affine_select(out=fold[:, :], in_=fold[:, :], compare_op=ALU.not_equal, fill=1.0,
                                    base=0, pattern=[[-1, K]], channel_multiplier=1).then_inc(cleared, 1)
            pool.wait_ge(cleared, 3)
            nc.gpsimd.affine_select(out=fold[:, :], in_=fold[:, :], compare_op=ALU.not_equal, fill=1.0,
                                    base=-K, pattern=[[-1, K]], channel_multiplier=1).then_inc(consts, 1)
            for m in range(MC):
                pool.wait_ge(b_landed[m], 16)
                if m >= 2:
                    pool.wait_ge(prep_ps, 2 * PREP.index(("B", m - 2)) + 2)
                nc.gpsimd.tensor_copy(b_order[:, m % 2, :, :, :],
                                      b_stage[:, m, :, :].rearrange("p k (j r) -> p j k r", r=R)
                                      ).then_inc(b_ordered, 1)

        @block.scalar
        def _(act):
            def router_hi(i):
                act.wait_ge(wr_ps, i + 1)
                nc.scalar.activation(wr_t[:, i * JB:(i + 1) * JB, 0:K],
                                     hb[:, i, :].rearrange("p (j q) -> p j q", j=JB)[:, :, 0:K],
                                     ACT.Copy).then_inc(wr_hid, 1)

            def weights_hi(n):
                kind, m = PREP[n]
                for half in range(2):
                    q = 2 * n + half
                    act.wait_ge(prep_ps, q + 1)
                    hi, _, order = turned(kind, m, half)
                    nc.scalar.activation(hi, ob[:, q % OSLOTS, :].rearrange(order, j=JB),
                                         ACT.Copy).then_inc(prep_hi, 1)

            def y_hi_part(g, c):
                act.wait_ge(y_ps, DC * g + (c + 1))
                nc.scalar.activation(y_hi[:, c, :], ob[:, c % OSLOTS, :], ACT.Copy).then_inc(y_hid, 1)

            def split_hi(g, u):
                t, ms = u // UPT, (u % UPT) * UM
                act.wait_ge(p_done, MC * g + (ms + UM))
                if not isinstance(g, int) or g > 0 or u >= SPLITS:
                    act.wait_ge(sp_used, UNITS * g + (u + 1 - SPLITS))
                nc.scalar.activation(ps_hi[:, u % SPLITS, :, :], p_t[:, ms:ms + UM, t * P:(t + 1) * P],
                                     ACT.Copy).then_inc(sp_hi, 1)

            def scores_out(g):
                act.wait_ge(s_ps, g + 1)
                if not isinstance(g, int) or g > 0:
                    for m in range(MC):
                        act.wait_ge(gx_landed[m], 32 * g)
                nc.scalar.activation(sg[:, :], sb_bank[:, :], ACT.Copy).then_inc(s_out, 1)

            def exponentials(g):
                act.wait_ge(topk, STEPS * g + BELOW)
                nc.scalar.activation(below[:, :, :], below[:, :, :], ACT.Exp).then_inc(exp_done, 1)

            def gates_out(g):
                act.wait_ge(gt_ps, g + 1)
                nc.scalar.activation(sg[:, 0:2 * P], sb_bank[:, 0:2 * P], ACT.Copy).then_inc(gt_out, 1)

            def steady(g, ahead):
                for c in range(DC):
                    if ahead:
                        y_hi_part(g + 1, c)
                    if c < SPLITS:
                        split_hi(g, c)
                if ahead:
                    scores_out(g + 1)
                for u in range(UNITS):
                    if u + SPLITS < UNITS:
                        split_hi(g, u + SPLITS)
                    if ahead and u == 4:
                        exponentials(g + 1)
                    if ahead and u == 8:
                        gates_out(g + 1)

            for i in range(WR_BANKS):
                router_hi(i)
            for c in range(DC):
                y_hi_part(0, c)
            weights_hi(0)
            scores_out(0)
            weights_hi(1)
            weights_hi(2)
            exponentials(0)
            weights_hi(3)
            gates_out(0)
            for n in range(EARLY, len(PREP)):
                weights_hi(n)
            steady(0, True)
            with act.Fori(1, NG - 1) as g:
                steady(g, True)
            steady(NG - 1, False)

        @block.vector
        def _(dve):
            def router_lo(i):
                dve.wait_ge(wr_hid, i + 1)
                cs = slice(i * JB, (i + 1) * JB)
                nc.vector.tensor_tensor(wr_t[:, cs, K:2 * K],
                                        hb[:, i, :].rearrange("p (j q) -> p j q", j=JB)[:, :, K:2 * K],
                                        wr_t[:, cs, 0:K].bitcast(F32), ALU.subtract).then_inc(wr_lod, 1)

            def weights_lo(n):
                kind, m = PREP[n]
                for half in range(2):
                    q = 2 * n + half
                    dve.wait_ge(prep_hi, q + 1)
                    hi, lo, order = turned(kind, m, half)
                    nc.vector.tensor_tensor(lo, ob[:, q % OSLOTS, :].rearrange(order, j=JB),
                                            hi.bitcast(F32), ALU.subtract).then_inc(prep_lo, 1)

            def y_lo_part(g, c):
                dve.wait_ge(y_hid, DC * g + (c + 1))
                nc.vector.tensor_tensor(y_lo[:, c, :], ob[:, c % OSLOTS, :], y_hi[:, c, :].bitcast(F32),
                                        ALU.subtract).then_inc(y_lod, 1)

            def gate_rows(g, m):
                dve.wait_ge(gx_landed[m], 32 * (g + 1))
                dve.wait_ge(h_ps, MC * g + (m + 1))
                nc.vector.tensor_tensor(p_t[:, m, :], hb[:, m % 2, :], p_t[:, m, :],
                                        ALU.mult).then_inc(p_done, 1)

            def split_lo(g, u):
                t, ms = u // UPT, (u % UPT) * UM
                dve.wait_ge(sp_hi, UNITS * g + (u + 1))
                nc.vector.tensor_tensor(ps_lo[:, u % SPLITS, :, :], p_t[:, ms:ms + UM, t * P:(t + 1) * P],
                                        ps_hi[:, u % SPLITS, :, :].bitcast(F32),
                                        ALU.subtract).then_inc(sp_lo, 1)

            def add_residual(g, k):
                slot = k % OSLOTS
                if k % HALVES == 0:
                    dve.wait_ge(o_ps, TILES * g + (k // HALVES + 1))
                else:
                    dve.wait_ge(sp_used, UNITS * g + UPT * (k // HALVES + 1))
                dve.wait_ge(r_landed[slot], 16 * ((OUTS // OSLOTS) * g + (k // OSLOTS + 1)))
                nc.vector.scalar_tensor_tensor(out=io[:, slot, :], in0=ob[:, slot, :], scalar=SCALING,
                                               in1=io[:, slot, :], op0=ALU.mult,
                                               op1=ALU.add).then_inc(o_done, 1)

            scores = tr_bank[:, 0:TILES * K].rearrange("p (t k) -> p t k", k=K)

            def per_row(a):
                return a.unsqueeze(2).broadcast_to([P, TILES, K])

            def gating(g, step):
                if step == MAX1:
                    dve.wait_ge(st_ps, g + 1)
                    nc.vector.tensor_copy(rows[:, :, :], scores)
                    dve.drain()
                    for t in range(TILES):
                        last = nc.vector.max(max1[:, t, :], rows[:, t, :])
                elif step == REST1:
                    dve.drain()
                    for t in range(TILES):
                        last = nc.vector.match_replace(rest1[:, t, :], max1[:, t, :], rows[:, t, :], LOWEST)
                elif step == MAX2:
                    dve.drain()
                    for t in range(TILES):
                        last = nc.vector.max(max2[:, t, :], rest1[:, t, :])
                elif step == REST2:
                    dve.drain()
                    for t in range(TILES):
                        last = nc.vector.match_replace(rest2[:, t, :], max2[:, t, :], rest1[:, t, :], LOWEST)
                elif step == BELOW:
                    last = nc.vector.tensor_tensor(below[:, :, :], rows[:, :, :], per_row(max1[:, :, 0]), ALU.subtract)
                elif step == CHOSEN:
                    dve.wait_ge(topk, STEPS * g + REST2)
                    last = nc.vector.tensor_tensor(rest2[:, :, :], rest2[:, :, :], rows[:, :, :], ALU.is_lt)
                elif step == WEIGHTED:
                    dve.wait_ge(exp_done, g + 1)
                    dve.wait_ge(topk, STEPS * g + CHOSEN)
                    last = nc.vector.tensor_tensor(below[:, :, :], below[:, :, :], rest2[:, :, :], ALU.mult)
                elif step == SUMMED:
                    dve.wait_ge(topk, STEPS * g + WEIGHTED)
                    last = nc.vector.reduce_sum(gsum[:, :], below[:, :, :], AX_X)
                elif step == INVERTED:
                    dve.wait_ge(topk, STEPS * g + SUMMED)
                    last = nc.vector.reciprocal(ginv[:, :], gsum[:, :])
                elif step == GATED:
                    dve.wait_ge(topk, STEPS * g + INVERTED)
                    last = nc.vector.tensor_tensor(
                        gates_n[:, :, :].rearrange("p (b a) k -> p a b k", a=2),
                        below[:, :, :].rearrange("p (a b) k -> p a b k", a=2),
                        per_row(ginv[:, :]).rearrange("p (a b) k -> p a b k", a=2), ALU.mult)
                last.then_inc(topk, 1)

            def steady(g, ahead, gated=False):
                if not gated:
                    for m in range(MC):
                        gate_rows(g, m)
                for c in range(DC):
                    if ahead:
                        y_lo_part(g + 1, c)
                    if c < SPLITS:
                        split_lo(g, c)
                for u in range(UNITS):
                    if u + SPLITS < UNITS:
                        split_lo(g, u + SPLITS)
                    if ahead and 2 <= u <= 6:
                        gating(g + 1, 2 * (u - 2) + 1)
                        gating(g + 1, 2 * (u - 2) + 2)
                    if u % UPT == UPT - 1:
                        for half in range(HALVES):
                            add_residual(g, HALVES * (u // UPT) + half)

            nc.vector.memset(w_diag[:, :, :], 0.0).then_inc(w_zeroed, 1)
            for i in range(WR_BANKS):
                router_lo(i)
            for c in range(DC):
                y_lo_part(0, c)
            weights_lo(0)
            weights_lo(1)
            for step in range(1, CHOSEN + 1):
                gating(0, step)
            weights_lo(2)
            for step in range(CHOSEN + 1, STEPS + 1):
                gating(0, step)
            weights_lo(3)
            for m in range(MC):
                for n in range(EARLY + 2 * m, min(EARLY + 2 * m + 2, len(PREP))):
                    weights_lo(n)
                gate_rows(0, m)
            steady(0, True, gated=True)
            with dve.Fori(1, NG - 1) as g:
                steady(g, True)
            steady(NG - 1, False)

        @block.tensor
        def _(pe):
            def turn_router(i):
                for j in range(JB):
                    c = i * JB + j
                    last = nc.tensor.transpose(hb[:, i, j * P:(j + 1) * P], wr_stage[:, c * P:(c + 1) * P],
                                               ident[:, :])
                last.then_inc(wr_ps, 1)

            def turn_weights(n):
                kind, m = PREP[n]
                if kind == "A":
                    pe.wait_ge(a_landed[m], 16)
                else:
                    pe.wait_ge(b_ordered, m + 1)
                for half in range(2):
                    q = 2 * n + half
                    if q < OSLOTS:
                        pe.wait_ge(y_lod, DC - OSLOTS + q + 1)
                    else:
                        pe.wait_ge(prep_lo, q - OSLOTS + 1)
                    for j in range(JB):
                        c = half * JB + j
                        src = a_stage[:, m, c * P:(c + 1) * P] if kind == "A" else \
                            b_order[:, m % 2, c, :, :].rearrange("p k r -> p (k r)")
                        last = nc.tensor.transpose(ob[:, q % OSLOTS, j * P:(j + 1) * P], src, ident[:, :])
                    last.then_inc(prep_ps, 1)

            def condition(g, c):
                pair = c // 2
                if c == 0:
                    pe.wait_ge(w_landed, 16 * TILES * BPT * (g + 1))
                if c % 2 == 0:
                    pe.wait_ge(x_landed[pair], 16 * (g + 1))
                if c >= OSLOTS:
                    pe.wait_ge(y_lod, DC * g + (c + 1 - OSLOTS))
                elif not isinstance(g, int) or g > 1:
                    pe.wait_ge(o_done, OUTS * g - OUTS + (c + 1 - OSLOTS))
                for t in range(TILES):
                    last = nc.tensor.matmul(ob[:, c % OSLOTS, t * P:(t + 1) * P],
                                            x_in[:, pair, t, (c % 2) * P:(c % 2 + 1) * P],
                                            w_diag[:, t, :], start=True, stop=True)
                last.then_inc(y_ps, 1)

            def route(g, c):
                pe.wait_ge(y_hid, DC * g + (c + 1))
                if c == 0 and (not isinstance(g, int) or g > 0):
                    pe.wait_ge(gt_out, g)
                nc.tensor.matmul(sb_bank[:, :], wr_t[:, c, :], y_hi[:, c, :], start=(c == 0), stop=False)
                pe.wait_ge(y_lod, DC * g + (c + 1))
                last = nc.tensor.matmul(sb_bank[:, :], wr_t[:, c, :], y_lo[:, c, :], start=False,
                                        stop=(c == DC - 1))
                if c == DC - 1:
                    last.then_inc(s_ps, 1)

            def condition_and_route(g, between):
                LAG = 2
                for c in range(DC):
                    condition(g, c)
                    if c >= LAG:
                        route(g, c - LAG)
                between()
                for c in range(DC - LAG, DC):
                    route(g, c)

            def scores_by_rows(g):
                pe.wait_ge(s_out, g + 1)
                for t in range(TILES):
                    last = nc.tensor.matmul(tr_bank[:, t * K:(t + 1) * K], sg[:, t * P:(t + 1) * P], fold[:, :],
                                            start=True, stop=True)
                last.then_inc(st_ps, 1)

            def turn_gates(g):
                pe.wait_ge(topk, STEPS * (g + 1))
                for t in range(2):
                    last = nc.tensor.transpose(sb_bank[:, t * P:(t + 1) * P], 
                                               gates_n[:, 2 * t:2 * t + 2, :].rearrange("p t k -> p (t k)"),
                                               ident[:, :])
                last.then_inc(gt_ps, 1)

            def up(g, m):
                n = MC * g + m
                if not isinstance(n, int) or n >= 2:
                    pe.wait_ge(p_done, n - 1)
                ms = slice(m * P, (m + 1) * P)
                for c in range(DC):
                    for i, (w, y) in enumerate(((a_lo, y_hi), (a_hi, y_lo), (a_hi, y_hi))):
                        last = nc.tensor.matmul(hb[:, m % 2, :], w[:, c, ms], y[:, c, :],
                                                start=(c == 0 and i == 0), stop=(c == DC - 1 and i == 2))
                last.then_inc(h_ps, 1)

            def down(g, u):
                t, mu, slot = u // UPT, u % UPT, u % SPLITS
                pe.wait_ge(sp_lo, UNITS * g + (u + 1))
                for half in range(HALVES):
                    k = HALVES * t + half
                    if mu == 0 and (not isinstance(g, int) or OUTS * g + k >= OSLOTS):
                        pe.wait_ge(o_done, OUTS * g + (k + 1 - OSLOTS))
                    ds = slice(half * BANK, (half + 1) * BANK)
                    for i in range(UM):
                        m = mu * UM + i
                        for j, (p, b) in enumerate(((ps_lo, b_hi), (ps_hi, b_lo), (ps_hi, b_hi))):
                            last = nc.tensor.matmul(ob[:, k % OSLOTS, :], p[:, slot, i, :], b[:, m, ds],
                                                    start=(m == 0 and j == 0), stop=(m == MC - 1 and j == 2))
                    if mu == UPT - 1 and half == 0:
                        last.then_inc(o_ps, 1)
                last.then_inc(sp_used, 1)

            def steady(g, ahead, upped=False):
                if not upped:
                    for m in range(MC):
                        up(g, m)
                if ahead:
                    condition_and_route(g + 1, lambda: down(g, 0))
                else:
                    down(g, 0)
                for u in range(1, UNITS):
                    down(g, u)
                    if ahead and u == 1:
                        scores_by_rows(g + 1)
                    if ahead and u == 7:
                        turn_gates(g + 1)

            pe.wait_ge(consts, 2)
            pe.wait_ge(wr_landed, 32)
            for i in range(WR_BANKS):
                turn_router(i)
            pe.wait_ge(wr_lod, WR_BANKS)
            condition_and_route(0, lambda: turn_weights(0))
            turn_weights(1)
            scores_by_rows(0)
            turn_weights(2)
            turn_weights(3)
            for m in range(MC):
                if m > 0:
                    for n in range(EARLY + 2 * (m - 1), min(EARLY + 2 * m, len(PREP))):
                        turn_weights(n)
                pe.wait_ge(prep_lo, 2 * PREP.index(("A", m)) + 2)
                up(0, m)
                if m == 0:
                    turn_gates(0)
            pe.wait_ge(prep_lo, N_PREP)
            steady(0, True, upped=True)
            with pe.Fori(1, NG - 1) as g:
                steady(g, True)
            steady(NG - 1, False)


_INS = ["x", "itok_B_0_15", "L0_cond_weights", "L0_ffn_A", "L0_ffn_B", "L0_ffn_Wr"]


def kernel(**inputs):
    import numpy as _np
    import concourse.bacc as _bacc
    from concourse import mybir as _mybir
    from concourse.bass_utils import run_bass_kernel_spmd as _run

    nc = _bacc.Bacc("TRN2", target_bir_lowering=False, num_devices=1, dynamic_dma_scratch_size=1024)
    arrays, args = {}, []
    for name in _INS:
        a = _np.ascontiguousarray(inputs[name])
        arrays[f"in_{name}"] = a
        args.append(nc.dram_tensor(f"in_{name}", a.shape, _mybir.dt.from_np(a.dtype), kind="ExternalInput").ap())
    out = nc.dram_tensor("out", inputs["x"].shape, _mybir.dt.float32, kind="ExternalOutput").ap()
    conditioned_moe_kernel(nc, *args, out)
    r = _run(nc, [arrays], core_ids=[0])
    return r.results[0]["out"]
```
